# Optimizing a Trainium2 kernel written in Bass

```python
import numpy as np
import jax
import jax.numpy as jnp

def _softmax(x, axis=-1):
    return jax.nn.softmax(x, axis=axis)

def _gelu(x):
    return jax.nn.gelu(x, approximate=True)

def _silu(x):
    return jax.nn.silu(x)

def _sigmoid(x):
    return jax.nn.sigmoid(x)

def _layernorm(x, axis=-1, eps=1e-05):
    m = jnp.mean(x, axis=axis, keepdims=True)
    v = jnp.var(x, axis=axis, keepdims=True)
    return (x - m) / jnp.sqrt(v + eps)

def _scatter_add(tgt, idx, src, axis=0):
    return tgt.at[idx].add(src)

def _segment_sum(src, seg, n):
    return jax.ops.segment_sum(src, seg, n)
kernel_name = 'mk_adj_preln_d4_adj_r2_102520'

def setup_inputs(seed: int=0):
    np.random.seed(seed)
    _w = jnp.asarray

    def _rec_inputs():
        import jax
        import jax.numpy as jnp
        _gk = jax.random.key(seed)
        x = -0.000929 + 1 * jax.random.normal(jax.random.fold_in(_gk, 1), (3327, 128), jnp.float32)
        _a = jax.random.bernoulli(jax.random.fold_in(_gk, 2), 0.00240457, (3327, 3327))
        _a = jnp.logical_or(_a, jnp.eye(3327, dtype=bool))
        _af = _a.astype(jnp.float32)
        _af = _af / jnp.maximum(_af.sum(-1, keepdims=True), 1.0)
        adj = _af
        return (x, adj)
    x, adj = _rec_inputs()

    def _L0_gnn_setup():
        import jax, jax.numpy as jnp
        import numpy as np
        from jax import lax
        D_MODEL = 128
        D_STATE = 16
        D_CONV = 4
        EXPAND = 2
        D_INNER = EXPAND * D_MODEL
        DT_RANK = (D_MODEL + 15) // 16
        N = 2048
        EPS = 1e-05

        def _mamba(h, w_in, conv_w, conv_b, w_xp, w_dt, b_dt, A_log, D_skip, w_out):
            L = h.shape[0]
            xz = h @ w_in
            xc, z = (xz[:, :D_INNER], xz[:, D_INNER:])
            xpad = jnp.pad(xc, ((D_CONV - 1, 0), (0, 0)))
            xconv = sum((xpad[k:k + L] * conv_w[:, k] for k in range(D_CONV))) + conv_b
            u = jax.nn.silu(xconv)
            dbc = u @ w_xp
            dt = jax.nn.softplus(dbc[:, :DT_RANK] @ w_dt + b_dt)
            B = dbc[:, DT_RANK:DT_RANK + D_STATE]
            C = dbc[:, DT_RANK + D_STATE:]
            A = -jnp.exp(A_log)
            dA = jnp.exp(dt[:, :, None] * A[None])
            dBu = dt[:, :, None] * B[:, None, :] * u[:, :, None]

            def step(hst, inp):
                dAt, dBut, Ct = inp
                hst = dAt * hst + dBut
                return (hst, hst @ Ct)
            _, ys = lax.scan(step, jnp.zeros((D_INNER, D_STATE), h.dtype), (dA, dBu, C))
            y = ys + u * D_skip
            y = y * jax.nn.silu(z)
            return y @ w_out
        key = jax.random.key(seed)
        ks = jax.random.split(key, 16)
        x = jax.random.normal(ks[0], (N, D_MODEL), dtype=jnp.float32)
        a = jax.random.uniform(ks[1], (N, N), dtype=jnp.float32)
        adj = a / a.sum(axis=1, keepdims=True)
        s = lambda fi, fo: 1.0 / np.sqrt(fi)
        gcn_w = jax.random.uniform(ks[2], (D_MODEL, D_MODEL), jnp.float32, -s(D_MODEL, 0), s(D_MODEL, 0))
        gcn_b = jnp.zeros((D_MODEL,), jnp.float32)
        ln_g = jnp.ones((D_MODEL,), jnp.float32)
        ln_b = jnp.zeros((D_MODEL,), jnp.float32)
        w_in = jax.random.normal(ks[3], (D_MODEL, 2 * D_INNER), jnp.float32) * s(D_MODEL, 0)
        conv_w = jax.random.normal(ks[4], (D_INNER, D_CONV), jnp.float32) * s(D_CONV, 0)
        conv_b = jnp.zeros((D_INNER,), jnp.float32)
        w_xp = jax.random.normal(ks[5], (D_INNER, DT_RANK + 2 * D_STATE), jnp.float32) * s(D_INNER, 0)
        w_dt = jax.random.normal(ks[6], (DT_RANK, D_INNER), jnp.float32) * s(DT_RANK, 0)
        b_dt = jnp.log(jnp.expm1(jnp.exp(jax.random.uniform(ks[7], (D_INNER,), jnp.float32, np.log(0.001), np.log(0.1)))))
        A_log = jnp.log(jnp.broadcast_to(jnp.arange(1, D_STATE + 1, dtype=jnp.float32), (D_INNER, D_STATE)))
        D_skip = jnp.ones((D_INNER,), jnp.float32)
        w_out = jax.random.normal(ks[8], (D_INNER, D_MODEL), jnp.float32) * s(D_INNER, 0)
        return dict(x=x, adj=adj, gcn_w=gcn_w, gcn_b=gcn_b, ln_g=ln_g, ln_b=ln_b, w_in=w_in, conv_w=conv_w, conv_b=conv_b, w_xp=w_xp, w_dt=w_dt, b_dt=b_dt, A_log=A_log, D_skip=D_skip, w_out=w_out)
    _L0_gnn_all = _L0_gnn_setup()
    _L0_gnn_in = {k: v for k, v in _L0_gnn_all.items() if k in ('gcn_w', 'gcn_b', 'ln_g', 'ln_b', 'w_in', 'conv_w', 'conv_b', 'w_xp', 'w_dt', 'b_dt', 'A_log', 'D_skip', 'w_out')}
    del _L0_gnn_all

    def _L1_gnn_setup():
        import jax, jax.numpy as jnp
        import numpy as np
        N = 4096
        D_IN = 128
        D_OUT = 128
        key = jax.random.key(seed)
        k1, k2, k3 = jax.random.split(key, 3)
        x = jax.random.normal(k1, (N, D_IN), dtype=jnp.float32)
        adj = jax.random.uniform(k2, (N, N), dtype=jnp.float32)
        W = jax.random.normal(k3, (D_OUT, D_IN), dtype=jnp.float32) * (1.0 / np.sqrt(D_IN))
        return {'x': x, 'adj': adj, 'W': W}
    _L1_gnn_all = _L1_gnn_setup()
    _L1_gnn_in = {k: v for k, v in _L1_gnn_all.items() if k in ('W',)}
    del _L1_gnn_all

    def _L2_gnn_setup():
        import jax, jax.numpy as jnp
        import numpy as np
        N, H, HEADS = (2048, 128, 3)
        ALPHA = 0.2
        NEG_INF = -9000000000000000.0

        def _sign_adj(key, n, density):
            k1, k2 = jax.random.split(key)
            mask = jax.random.uniform(k1, (n, n)) < density
            sign = jnp.where(jax.random.uniform(k2, (n, n)) < 0.5, -1.0, 1.0)
            adj = jnp.where(mask, sign, 0.0).astype(jnp.float32)
            idx = jnp.arange(n)
            return adj.at[idx, idx].set(1.0)

        def _gru_cell(x, hstate, Wih, Whh, bih, bhh):
            gi = x @ Wih.T + bih
            gh = hstate @ Whh.T + bhh
            ir, iz, inn = jnp.split(gi, 3, axis=1)
            hr, hz, hn = jnp.split(gh, 3, axis=1)
            r = jax.nn.sigmoid(ir + hr)
            z = jax.nn.sigmoid(iz + hz)
            n = jnp.tanh(inn + r * hn)
            return (1.0 - z) * n + z * hstate

        def _gat_head(h, node_adj, edge_adj, W, a):
            hW = h @ W
            hp = (node_adj > 0).astype(hW.dtype) @ hW
            hm = (node_adj < 0).astype(hW.dtype) @ hW
            e_plus = jax.nn.leaky_relu(jnp.concatenate([hp, hm], axis=1) @ a, ALPHA)[:, 0]
            e_minus = jax.nn.leaky_relu(jnp.concatenate([hm, hp], axis=1) @ a, ALPHA)[:, 0]
            att = jnp.where(edge_adj > 0, e_plus[None, :], NEG_INF)
            att = jnp.where(edge_adj < 0, e_minus[None, :], att)
            att = jax.nn.softmax(att, axis=1)
            return att * edge_adj @ hW
        key = jax.random.key(seed)
        ks = jax.random.split(key, 16)
        std = 0.01
        gain = 1.414
        return {'h': jax.random.normal(ks[0], (N, H), jnp.float32), 'node_adj': _sign_adj(ks[1], N, 0.005), 'edge_adj': _sign_adj(ks[2], N, 0.005), 'gat_W': jax.random.normal(ks[3], (HEADS, H, H), jnp.float32) * (gain / np.sqrt(H, dtype=np.float32)), 'gat_a': jax.random.normal(ks[4], (HEADS, 2 * H, 1), jnp.float32) * 0.1, 'edge_Wih': jax.random.normal(ks[5], (3 * H, H), jnp.float32) * std, 'edge_Whh': jax.random.normal(ks[6], (3 * H, H), jnp.float32) * std, 'edge_bih': jnp.zeros((3 * H,), jnp.float32), 'edge_bhh': jnp.zeros((3 * H,), jnp.float32), 'node_Wih': jax.random.normal(ks[7], (3 * H, H), jnp.float32) * std, 'node_Whh': jax.random.normal(ks[8], (3 * H, H), jnp.float32) * std, 'node_bih': jnp.zeros((3 * H,), jnp.float32), 'node_bhh': jnp.zeros((3 * H,), jnp.float32)}
    _L2_gnn_all = _L2_gnn_setup()
    _L2_gnn_in = {k: v for k, v in _L2_gnn_all.items() if k in ('gat_W', 'gat_a', 'edge_Wih', 'edge_Whh', 'edge_bih', 'edge_bhh', 'node_Wih', 'node_Whh', 'node_bih', 'node_bhh')}
    del _L2_gnn_all

    def _L3_gnn_setup():
        import jax, jax.numpy as jnp
        import numpy as np
        D_IN = 128
        D_ATTN = 64
        STEPS = 2
        TOP_P = 0.9
        TAU = 1.0
        LN_EPS = 1e-05
        N_NODES = 4096

        def _top_p_attention(X, W1, W2, W3):
            q = X @ W1.T @ W2.T
            k = X @ W3.T
            logits = q @ k.T / TAU
            probs = jax.nn.softmax(logits, axis=-1)
            idx = jnp.argsort(-probs, axis=-1)
            sp = jnp.take_along_axis(probs, idx, axis=-1)
            cs = jnp.cumsum(sp, axis=-1)
            keep_sorted = cs - sp < TOP_P
            rows = jnp.arange(probs.shape[0])[:, None]
            mask = jnp.zeros(probs.shape, dtype=bool).at[rows, idx].set(keep_sorted)
            A = probs * mask
            return A / jnp.maximum(A.sum(-1, keepdims=True), 1e-12)
        key = jax.random.key(seed)
        ks = jax.random.split(key, 8)
        N, d, da, steps = (N_NODES, D_IN, D_ATTN, STEPS)
        X = jax.random.normal(ks[0], (N, d), dtype=jnp.float32)
        S = jax.random.uniform(ks[1], (N, N), dtype=jnp.float32)
        W1 = jax.random.normal(ks[2], (da, d), dtype=jnp.float32) / np.sqrt(d)
        W2 = jax.random.normal(ks[3], (da, da), dtype=jnp.float32) / np.sqrt(da)
        W3 = jax.random.normal(ks[4], (da, d), dtype=jnp.float32) / np.sqrt(d)
        U1 = jax.random.normal(ks[5], (steps, d, d), dtype=jnp.float32) / np.sqrt(d)
        U2 = jax.random.normal(ks[6], (steps, d, d), dtype=jnp.float32) / np.sqrt(d)
        ln_g = jnp.ones((d,), dtype=jnp.float32)
        ln_b = jnp.zeros((d,), dtype=jnp.float32)
        return {'X': X, 'S': S, 'W1': W1, 'W2': W2, 'W3': W3, 'U1': U1, 'U2': U2, 'ln_g': ln_g, 'ln_b': ln_b}
    _L3_gnn_all = _L3_gnn_setup()
    _L3_gnn_in = {k: v for k, v in _L3_gnn_all.items() if k in ('W1', 'W2', 'W3', 'U1', 'U2', 'ln_g', 'ln_b')}
    del _L3_gnn_all
    return {'x': x, 'adj': adj, 'L0_gnn_gcn_w': _L0_gnn_in['gcn_w'], 'L0_gnn_gcn_b': _L0_gnn_in['gcn_b'], 'L0_gnn_ln_g': _L0_gnn_in['ln_g'], 'L0_gnn_ln_b': _L0_gnn_in['ln_b'], 'L0_gnn_w_in': _L0_gnn_in['w_in'], 'L0_gnn_conv_w': _L0_gnn_in['conv_w'], 'L0_gnn_conv_b': _L0_gnn_in['conv_b'], 'L0_gnn_w_xp': _L0_gnn_in['w_xp'], 'L0_gnn_w_dt': _L0_gnn_in['w_dt'], 'L0_gnn_b_dt': _L0_gnn_in['b_dt'], 'L0_gnn_A_log': _L0_gnn_in['A_log'], 'L0_gnn_D_skip': _L0_gnn_in['D_skip'], 'L0_gnn_w_out': _L0_gnn_in['w_out'], 'L1_gnn_W': _L1_gnn_in['W'], 'L2_gnn_gat_W': _L2_gnn_in['gat_W'], 'L2_gnn_gat_a': _L2_gnn_in['gat_a'], 'L2_gnn_edge_Wih': _L2_gnn_in['edge_Wih'], 'L2_gnn_edge_Whh': _L2_gnn_in['edge_Whh'], 'L2_gnn_edge_bih': _L2_gnn_in['edge_bih'], 'L2_gnn_edge_bhh': _L2_gnn_in['edge_bhh'], 'L2_gnn_node_Wih': _L2_gnn_in['node_Wih'], 'L2_gnn_node_Whh': _L2_gnn_in['node_Whh'], 'L2_gnn_node_bih': _L2_gnn_in['node_bih'], 'L2_gnn_node_bhh': _L2_gnn_in['node_bhh'], 'L3_gnn_W1': _L3_gnn_in['W1'], 'L3_gnn_W2': _L3_gnn_in['W2'], 'L3_gnn_W3': _L3_gnn_in['W3'], 'L3_gnn_U1': _L3_gnn_in['U1'], 'L3_gnn_U2': _L3_gnn_in['U2'], 'L3_gnn_ln_g': _L3_gnn_in['ln_g'], 'L3_gnn_ln_b': _L3_gnn_in['ln_b']}

def reference(x, adj, L0_gnn_gcn_w, L0_gnn_gcn_b, L0_gnn_ln_g, L0_gnn_ln_b, L0_gnn_w_in, L0_gnn_conv_w, L0_gnn_conv_b, L0_gnn_w_xp, L0_gnn_w_dt, L0_gnn_b_dt, L0_gnn_A_log, L0_gnn_D_skip, L0_gnn_w_out, L1_gnn_W, L2_gnn_gat_W, L2_gnn_gat_a, L2_gnn_edge_Wih, L2_gnn_edge_Whh, L2_gnn_edge_bih, L2_gnn_edge_bhh, L2_gnn_node_Wih, L2_gnn_node_Whh, L2_gnn_node_bih, L2_gnn_node_bhh, L3_gnn_W1, L3_gnn_W2, L3_gnn_W3, L3_gnn_U1, L3_gnn_U2, L3_gnn_ln_g, L3_gnn_ln_b):
    import jax
    import jax.numpy as jnp

    def _L0_gnn_ref(x, adj, gcn_w, gcn_b, ln_g, ln_b, w_in, conv_w, conv_b, w_xp, w_dt, b_dt, A_log, D_skip, w_out):
        import jax, jax.numpy as jnp
        import numpy as np
        from jax import lax
        D_MODEL = 128
        D_STATE = 16
        D_CONV = 4
        EXPAND = 2
        D_INNER = EXPAND * D_MODEL
        DT_RANK = (D_MODEL + 15) // 16
        N = 2048
        EPS = 1e-05

        def _mamba(h, w_in, conv_w, conv_b, w_xp, w_dt, b_dt, A_log, D_skip, w_out):
            L = h.shape[0]
            xz = h @ w_in
            xc, z = (xz[:, :D_INNER], xz[:, D_INNER:])
            xpad = jnp.pad(xc, ((D_CONV - 1, 0), (0, 0)))
            xconv = sum((xpad[k:k + L] * conv_w[:, k] for k in range(D_CONV))) + conv_b
            u = jax.nn.silu(xconv)
            dbc = u @ w_xp
            dt = jax.nn.softplus(dbc[:, :DT_RANK] @ w_dt + b_dt)
            B = dbc[:, DT_RANK:DT_RANK + D_STATE]
            C = dbc[:, DT_RANK + D_STATE:]
            A = -jnp.exp(A_log)
            dA = jnp.exp(dt[:, :, None] * A[None])
            dBu = dt[:, :, None] * B[:, None, :] * u[:, :, None]

            def step(hst, inp):
                dAt, dBut, Ct = inp
                hst = dAt * hst + dBut
                return (hst, hst @ Ct)
            _, ys = lax.scan(step, jnp.zeros((D_INNER, D_STATE), h.dtype), (dA, dBu, C))
            y = ys + u * D_skip
            y = y * jax.nn.silu(z)
            return y @ w_out
        h = jax.nn.relu(adj @ x @ gcn_w + gcn_b)
        mu = h.mean(-1, keepdims=True)
        var = h.var(-1, keepdims=True)
        h = (h - mu) * lax.rsqrt(var + EPS) * ln_g + ln_b
        return _mamba(h, w_in, conv_w, conv_b, w_xp, w_dt, b_dt, A_log, D_skip, w_out)

    def _L1_gnn_ref(x, adj, W):
        import jax, jax.numpy as jnp
        import numpy as np
        N = 4096
        D_IN = 128
        D_OUT = 128
        A_hat = adj + jnp.eye(adj.shape[0], dtype=adj.dtype)
        d_inv_sqrt = jnp.sum(A_hat, axis=1) ** (-0.5)
        A_norm = d_inv_sqrt[:, None] * A_hat * d_inv_sqrt[None, :]
        support = x @ W.T
        out = A_norm @ support
        return jax.nn.relu(out)

    def _L2_gnn_ref(h, node_adj, edge_adj, gat_W, gat_a, edge_Wih, edge_Whh, edge_bih, edge_bhh, node_Wih, node_Whh, node_bih, node_bhh):
        import jax, jax.numpy as jnp
        import numpy as np
        N, H, HEADS = (2048, 128, 3)
        ALPHA = 0.2
        NEG_INF = -9000000000000000.0

        def _sign_adj(key, n, density):
            k1, k2 = jax.random.split(key)
            mask = jax.random.uniform(k1, (n, n)) < density
            sign = jnp.where(jax.random.uniform(k2, (n, n)) < 0.5, -1.0, 1.0)
            adj = jnp.where(mask, sign, 0.0).astype(jnp.float32)
            idx = jnp.arange(n)
            return adj.at[idx, idx].set(1.0)

        def _gru_cell(x, hstate, Wih, Whh, bih, bhh):
            gi = x @ Wih.T + bih
            gh = hstate @ Whh.T + bhh
            ir, iz, inn = jnp.split(gi, 3, axis=1)
            hr, hz, hn = jnp.split(gh, 3, axis=1)
            r = jax.nn.sigmoid(ir + hr)
            z = jax.nn.sigmoid(iz + hz)
            n = jnp.tanh(inn + r * hn)
            return (1.0 - z) * n + z * hstate

        def _gat_head(h, node_adj, edge_adj, W, a):
            hW = h @ W
            hp = (node_adj > 0).astype(hW.dtype) @ hW
            hm = (node_adj < 0).astype(hW.dtype) @ hW
            e_plus = jax.nn.leaky_relu(jnp.concatenate([hp, hm], axis=1) @ a, ALPHA)[:, 0]
            e_minus = jax.nn.leaky_relu(jnp.concatenate([hm, hp], axis=1) @ a, ALPHA)[:, 0]
            att = jnp.where(edge_adj > 0, e_plus[None, :], NEG_INF)
            att = jnp.where(edge_adj < 0, e_minus[None, :], att)
            att = jax.nn.softmax(att, axis=1)
            return att * edge_adj @ hW
        dn = jnp.diag(node_adj)
        de = jnp.diag(edge_adj)
        idx = jnp.arange(node_adj.shape[0])
        node_adj_norm = node_adj.at[idx, idx].add(-dn)
        edge_adj_norm = edge_adj.at[idx, idx].add(-de)
        node_support = node_adj_norm @ h
        edge_output = _gru_cell(node_support, h, edge_Wih, edge_Whh, edge_bih, edge_bhh)
        edge_support = _gat_head(h, node_adj_norm, edge_adj_norm, gat_W[0], gat_a[0])
        for i in range(1, HEADS):
            edge_support = edge_support + _gat_head(h, node_adj_norm, edge_adj_norm, gat_W[i], gat_a[i])
        edge_support = edge_support / HEADS
        node_output = _gru_cell(edge_support, h, node_Wih, node_Whh, node_bih, node_bhh)
        return de[:, None] * edge_output + dn[:, None] * node_output

    def _L3_gnn_ref(X, S, W1, W2, W3, U1, U2, ln_g, ln_b):
        import jax, jax.numpy as jnp
        import numpy as np
        D_IN = 128
        D_ATTN = 64
        STEPS = 2
        TOP_P = 0.9
        TAU = 1.0
        LN_EPS = 1e-05
        N_NODES = 4096

        def _top_p_attention(X, W1, W2, W3):
            q = X @ W1.T @ W2.T
            k = X @ W3.T
            logits = q @ k.T / TAU
            probs = jax.nn.softmax(logits, axis=-1)
            idx = jnp.argsort(-probs, axis=-1)
            sp = jnp.take_along_axis(probs, idx, axis=-1)
            cs = jnp.cumsum(sp, axis=-1)
            keep_sorted = cs - sp < TOP_P
            rows = jnp.arange(probs.shape[0])[:, None]
            mask = jnp.zeros(probs.shape, dtype=bool).at[rows, idx].set(keep_sorted)
            A = probs * mask
            return A / jnp.maximum(A.sum(-1, keepdims=True), 1e-12)
        N = X.shape[0]
        R = S + jnp.eye(N, dtype=X.dtype)
        R = R / R.sum(-1, keepdims=True)
        Z = jnp.zeros_like(X)
        Xf = X
        Xa = X
        for n in range(STEPS):
            A = _top_p_attention(Xa, W1, W2, W3)
            Xf = R @ Xf
            Xa = A @ Xa
            Z = Z + Xf @ U1[n].T + Xa @ U2[n].T
        h = X + Z
        mu = h.mean(-1, keepdims=True)
        var = jnp.mean((h - mu) ** 2, axis=-1, keepdims=True)
        return (h - mu) / jnp.sqrt(var + LN_EPS) * ln_g + ln_b
    h = jnp.maximum(_layernorm(x, axis=-1), 0.0)
    x = x + _L0_gnn_ref(h, adj, L0_gnn_gcn_w, L0_gnn_gcn_b, L0_gnn_ln_g, L0_gnn_ln_b, L0_gnn_w_in, L0_gnn_conv_w, L0_gnn_conv_b, L0_gnn_w_xp, L0_gnn_w_dt, L0_gnn_b_dt, L0_gnn_A_log, L0_gnn_D_skip, L0_gnn_w_out)
    h = jnp.maximum(_layernorm(x, axis=-1), 0.0)
    x = x + _L1_gnn_ref(h, adj, L1_gnn_W)
    h = jnp.maximum(_layernorm(x, axis=-1), 0.0)
    x = x + _L2_gnn_ref(h, adj, adj, L2_gnn_gat_W, L2_gnn_gat_a, L2_gnn_edge_Wih, L2_gnn_edge_Whh, L2_gnn_edge_bih, L2_gnn_edge_bhh, L2_gnn_node_Wih, L2_gnn_node_Whh, L2_gnn_node_bih, L2_gnn_node_bhh)
    h = jnp.maximum(_layernorm(x, axis=-1), 0.0)
    x = x + _L3_gnn_ref(h, adj, L3_gnn_W1, L3_gnn_W2, L3_gnn_W3, L3_gnn_U1, L3_gnn_U2, L3_gnn_ln_g, L3_gnn_ln_b)
    return x

_drawn_inputs = setup_inputs


def setup_inputs(seed=0):
    import zlib

    import numpy as np

    out = dict(_drawn_inputs(seed))
    spreads = {'L0_gnn_gcn_b': (0.0, 0.1),
     'L0_gnn_ln_g': (1.0, 0.2),
     'L0_gnn_ln_b': (0.0, 0.1),
     'L0_gnn_conv_b': (0.0, 0.1),
     'L0_gnn_D_skip': (1.0, 0.2),
     'L2_gnn_edge_bih': (0.0, 0.8),
     'L2_gnn_edge_bhh': (0.0, 2.0),
     'L2_gnn_node_bih': (0.0, 0.8),
     'L2_gnn_node_bhh': (0.0, 2.0),
     'L3_gnn_ln_g': (1.0, 0.2),
     'L3_gnn_ln_b': (0.0, 0.1)}
    factors = {'L0_gnn_w_dt': 5.95,
     'L0_gnn_b_dt': 3.174,
     'L2_gnn_gat_W': 8.0,
     'L2_gnn_gat_a': 8.0,
     'L2_gnn_edge_Wih': 24.575,
     'L2_gnn_edge_Whh': 22.117,
     'L2_gnn_node_Wih': 8.0,
     'L2_gnn_node_Whh': 22.692}
    for name, (base, spread) in spreads.items():
        noise = np.random.default_rng([zlib.crc32(name.encode()), seed]).standard_normal(out[name].shape)
        drawn = base * np.exp(spread * noise) if base else spread * noise
        out[name] = jnp.asarray(drawn.astype(out[name].dtype))
    for name, factor in factors.items():
        out[name] = (out[name] * factor).astype(out[name].dtype)
    return out
```

```python
from contextlib import ExitStack, contextmanager

import concourse.bass as bass
from concourse import mybir

F32 = mybir.dt.float32
BF16 = mybir.dt.bfloat16
I32 = mybir.dt.int32
ACT = mybir.ActivationFunctionType
ALU = mybir.AluOpType
AX = mybir.AxisListType.X
ds = bass.ds

N = 3327
P = 128
T = (N + P - 1) // P
NP = T * P
CW = 416
NCH = NP // CW
PW = 2 * P
NPC = NP // PW
BANK = 512
GROUPS = [(g, min(4, T - 4 * g)) for g in range((T + 3) // 4)]
DI = 256
DS = 16
DR = 8
HEADS = 3
DA = 64
MASKED = -9e15
TOP_P = 0.9
SEARCH = 24


class Kept:
    pass


class Stage:

    def __init__(self, nc, name, ctx):
        self.nc, self.name, self.ctx, self.all, self.block = nc, name, ctx, [], None

    def sb(self, what, shape, dt=F32):
        return self.ctx.enter_context(self.nc.sbuf_tensor(f"{self.name}_{what}", shape, dt))

    def ps(self, what, shape, dt=F32):
        return self.ctx.enter_context(self.nc.psum_tensor(f"{self.name}_{what}", shape, dt))

    def sem(self, what):
        self.all.append(self.nc.alloc_semaphore(name=f"{self.name}_{what}"))
        return self.all[-1]

    def sems(self, what, n):
        return [self.sem(f"{what}{b}") for b in range(n)]


class Counter:

    def __init__(self, eng, sem):
        self.eng, self.sem, self.base, self.n, self.outer = eng, sem, 0, 0, []

    def __call__(self, op):
        op.then_inc(self.sem, 1)
        self.n += 1
        self.eng.wait_ge(self.sem, self.base + self.n)

    @contextmanager
    def loop(self, rounds, per):
        with self.eng.Fori(0, rounds) as i:
            self.outer.append((self.base, self.n))
            self.base, self.n = self.base + self.n + i * per, 0
            yield i
            assert self.n == per, f"a round counts {self.n}, not {per}"
        base, n = self.outer.pop()
        self.base, self.n = base, n + rounds * per


def signal(eng, op, sem, value):
    op.then_inc(sem, 1)
    eng.wait_ge(sem, value + 1)


def opens(eng, *sems):
    for s in sems:
        for one in s if isinstance(s, (list, tuple)) else (s,):
            eng.sem_inc(one, 1)


def apart(eng):
    eng.nop(nofuse=True)


@contextmanager
def stage(nc, name):
    with ExitStack() as ctx:
        st = Stage(nc, name, ctx)
        with nc.Block() as st.block:
            yield st
        nc.clear_and_free_semaphores(st.all)
        nc.all_engine_barrier()


def pairs(eng, count, body):
    with eng.Fori(0, count // 2) as i:
        body(i, 0)
        body(i, 1)
    if count % 2:
        body(count // 2, 0)


def layer_norm(nc, k, name, src, dst, relu, scale=None, shift=None):
    with stage(nc, name) as st:
        mean, var = st.ps("mean", [P, 2, BANK]), st.ps("var", [P, 2, BANK])
        xc, sq, sd, rs = (st.sb(w, [P, 2, CW]) for w in ("xc", "sq", "sd", "rs"))
        s_mean, s_xc, s_sq, s_var, s_sd, s_out = (st.sems(w, 2) for w in ("mean", "xc", "sq", "var", "sd", "out"))
        s_v = st.sem("v")

        def cols(i, b):
            return ds((2 * i + b) * CW, CW)

        @st.block.tensor
        def _(pe):
            opens(pe, s_mean, s_var)
            with pe.Fori(0, NCH // 2) as i:
                for b in range(2):
                    pe.wait_ge(s_xc[b], i + 1)
                    pe.matmul(mean[:, b, :CW], k.avg[:], src[:, cols(i, b)], start=True, stop=True).then_inc(s_mean[b], 1)
                for b in range(2):
                    pe.wait_ge(s_sq[b], i + 2)
                    pe.wait_ge(s_sd[b], i + 1)
                    pe.matmul(var[:, b, :CW], k.avg[:], sq[:, b, :], start=True, stop=True).then_inc(s_var[b], 1)

        @st.block.vector
        def _(v):
            opens(v, s_xc, s_out)
            own = Counter(v, s_v)
            per = 2 if relu else 6
            with own.loop(NCH // 2, per) as i:
                for b in range(2):
                    v.wait_ge(s_mean[b], i + 2)
                    signal(v, v.tensor_tensor(xc[:, b, :], src[:, cols(i, b)], mean[:, b, :CW], ALU.subtract), s_xc[b], i + 1)
                for b in range(2):
                    v.wait_ge(s_sd[b], i + 2)
                    own(v.reciprocal(rs[:, b, :], sd[:, b, :]))
                    if relu:
                        op = v.scalar_tensor_tensor(dst[:, cols(i, b)], xc[:, b, :], 0.0, rs[:, b, :], ALU.max, ALU.mult)
                    else:
                        own(v.tensor_tensor(xc[:, b, :], xc[:, b, :], rs[:, b, :], ALU.mult))
                        own(v.tensor_scalar(xc[:, b, :], xc[:, b, :], scale, None, ALU.mult))
                        op = v.tensor_scalar(dst[:, cols(i, b)], xc[:, b, :], shift, None, ALU.add)
                    signal(v, op, s_out[b], i + 1)

        @st.block.scalar
        def _(a):
            opens(a, s_sq, s_sd)
            with a.Fori(0, NCH // 2) as i:
                for b in range(2):
                    a.wait_ge(s_xc[b], i + 2)
                    a.wait_ge(s_var[b], i + 1)
                    signal(a, a.activation(sq[:, b, :], xc[:, b, :], ACT.Square), s_sq[b], i + 1)
                for b in range(2):
                    a.wait_ge(s_var[b], i + 2)
                    a.wait_ge(s_out[b], i + 1)
                    signal(a, a.activation(sd[:, b, :], var[:, b, :CW], ACT.Sqrt, bias=k.eps[:]), s_sd[b], i + 1)


def by_tiles(nc, name, emit, place, width=P, scale=None):
    with stage(nc, name) as st:
        ps = st.ps("ps", [P, len(GROUPS), BANK])
        s_full, s_out = st.sems("full", len(GROUPS)), st.sems("out", 2)

        @st.block.tensor
        def _(pe):
            opens(pe, s_full)
            for g, n in GROUPS:
                for q in range(n):
                    op = emit(pe, ps[:, g, q * width:(q + 1) * width], 4 * g + q)
                op.then_inc(s_full[g], 1)

        def copies(eng, who):
            opens(eng, s_out[who])
            count = 0
            for g, n in GROUPS:
                if g % 2 != who:
                    continue
                eng.wait_ge(s_full[g], 2)
                out = place(g, n)
                for q in range(n if scale else 1):
                    src = ps[:, g, q * width:(q + 1) * width] if scale else ps[:, g, 0:n * width]
                    dst = out[:, q * width:(q + 1) * width] if scale else out
                    s = scale(4 * g + q) if scale else 1.0
                    op = (eng.tensor_scalar(dst, src, s, None, ALU.mult) if who == 0 else
                          eng.activation(dst, src, ACT.Copy, scale=s))
                    op.then_inc(s_out[who], 1)
                    count += 1
            eng.wait_ge(s_out[who], count + 1)

        st.block.vector(lambda v: copies(v, 0))
        st.block.scalar(lambda a: copies(a, 1))


def rows_of(R):
    flat = R if len(R.shape) == 2 else R[:].rearrange("p t d -> p (t d)")
    return lambda g, n: flat[:, 4 * g * P:(4 * g + n) * P]


def to_rows(nc, k, name, src, dst):
    by_tiles(nc, name, lambda pe, out, t: pe.transpose(out, src[:, t * P:(t + 1) * P], k.ident[:]), rows_of(dst))


def to_cols(nc, k, name, src, dst):
    by_tiles(nc, name, lambda pe, out, t: pe.transpose(out, src[:, t, :], k.ident[:]), rows_of(dst))


def rows_times(nc, k, name, src, w, dst, scale=None):
    by_tiles(nc, name, lambda pe, out, t: pe.matmul(out, src[:, t * P:(t + 1) * P], w, start=True, stop=True),
             rows_of(dst), scale=scale)


def spread(nc, k, name, vec, dst):
    with stage(nc, name) as st:
        diag = st.sb("diag", [P, T, P])
        ps = st.ps("ps", [P, len(GROUPS), BANK])
        s_diag, s_full, s_out = st.sem("diag"), st.sem("full"), st.sem("out")

        @st.block.vector
        def _(v):
            opens(v, s_diag)
            for t in range(T):
                v.tensor_scalar(diag[:, t, :], k.ident[:], vec[:, t:t + 1], None, ALU.mult).then_inc(s_diag, 1)

        @st.block.tensor
        def _(pe):
            opens(pe, s_full)
            for g, n in GROUPS:
                pe.wait_ge(s_diag, 4 * g + n + 1)
                pe.matmul(ps[:, g, 0:n * P], k.ones[:], diag[:, 4 * g:4 * g + n, :], start=True, stop=True).then_inc(s_full, 1)

        @st.block.scalar
        def _(a):
            opens(a, s_out)
            for g, n in GROUPS:
                a.wait_ge(s_full, g + 2)
                a.activation(rows_of(dst)(g, n), ps[:, g, 0:n * P], ACT.Copy).then_inc(s_out, 1)
            a.wait_ge(s_out, len(GROUPS) + 1)


WEIGHTS = ["L1_gnn_W", "L2_gnn_gat_W", "L2_gnn_edge_Wih", "L2_gnn_edge_Whh", "L2_gnn_node_Wih", "L2_gnn_node_Whh",
           "L3_gnn_U1", "L3_gnn_U2"]
NW = 23
AT_GAT, AT_EDGE, AT_NODE, AT_U1, AT_U2, AT_W1, AT_W2, AT_W3 = 1, 4, 10, 16, 18, 20, 21, 22
VECS = [("L0_gnn_gcn_b", 1), ("L0_gnn_ln_g", 1), ("L0_gnn_ln_b", 1), ("L3_gnn_ln_g", 1), ("L3_gnn_ln_b", 1),
        ("L0_gnn_conv_b", 2), ("L0_gnn_b_dt", 2), ("L0_gnn_D_skip", 2),
        ("L2_gnn_edge_bih", 3), ("L2_gnn_edge_bhh", 3), ("L2_gnn_node_bih", 3), ("L2_gnn_node_bhh", 3)]


def vec_columns():
    at, found = 0, {}
    for name, n in VECS:
        found[name] = at
        at += n
    return found, at


VCOL, NVEC = vec_columns()


def setup(nc, k, d):
    with stage(nc, "setup") as st:
        xr = st.sb("xr", [P, T, P])
        wr = st.sb("wr", [P, NW, P])
        gata = st.sb("gata", [P, HEADS, 2])
        ps = st.ps("ps", [P, 7, BANK])
        small = st.ps("small", [P, 2 * HEADS])
        s_c, s_x, s_w, s_v, s_m = st.sem("const"), st.sem("x"), st.sem("w"), st.sem("vec"), st.sem("m")
        s_t, s_copy, s_wa, s_own, s_a = st.sem("t"), st.sem("copy"), st.sem("wa"), st.sem("own"), st.sem("act")
        full = N // P
        n_w = [0]

        @st.block.sync
        def _(sp):
            opens(sp, s_x, s_w)
            sp.wait_ge(s_m, 2)
            x = d["x"]
            sp.dma_start(xr[:, 0:full, :], x[0:full * P, :].rearrange("(t p) d -> p t d", p=P)).then_inc(s_x, 16)
            sp.dma_start(xr[0:N - full * P, full, :], x[full * P:N, :]).then_inc(s_x, 16)
            sp.dma_start(gata[:], d["L2_gnn_gat_a"].rearrange("h (a p) o -> p h (a o)", p=P),
                         allow_slow_non_contiguous=True).then_inc(s_w, 16)
            at = 0
            for name in WEIGHTS:
                w = d[name]
                w = w.rearrange("h (g p) c -> p (h g) c", p=P) if len(w.shape) == 3 else w.rearrange("(g p) c -> p g c", p=P)
                sp.dma_start(wr[:, at:at + w.shape[1], :], w).then_inc(s_w, 16)
                at += w.shape[1]
            assert at == AT_W1
            sp.dma_start(wr[0:DA, AT_W1, :], d["L3_gnn_W1"]).then_inc(s_w, 16)
            sp.dma_start(wr[0:DA, AT_W2, 0:DA], d["L3_gnn_W2"]).then_inc(s_w, 16)
            sp.dma_start(wr[0:DA, AT_W3, :], d["L3_gnn_W3"]).then_inc(s_w, 16)
            n_w[0] = 16 * (len(WEIGHTS) + 4)
            sp.wait_ge(s_x, 33)
            sp.wait_ge(s_w, n_w[0] + 1)

        @st.block.scalar
        def _(a):
            opens(a, s_v, s_a)
            loads = [(k.vec[:, VCOL[name]:VCOL[name] + n], d[name].rearrange("(g p) -> p g", p=P)) for name, n in VECS]
            loads += [(k.convw[:], d["L0_gnn_conv_w"].rearrange("(g p) c -> p g c", p=P)),
                      (k.alog[:], d["L0_gnn_A_log"].rearrange("(g p) c -> p g c", p=P)),
                      (k.gcnw[:], d["L0_gnn_gcn_w"]), (k.win[:], d["L0_gnn_w_in"]),
                      (k.wxp[:], d["L0_gnn_w_xp"].rearrange("(g p) c -> p g c", p=P)),
                      (k.wdt[:], d["L0_gnn_w_dt"]),
                      (k.wout[:], d["L0_gnn_w_out"].rearrange("(g p) c -> p g c", p=P)),
                      (k.gatw[:], d["L2_gnn_gat_W"].rearrange("h p c -> p h c"))]
            for out, src in loads:
                a.dma_start(out, src, allow_slow_non_contiguous=True).then_inc(s_v, 16)
            a.wait_ge(s_v, 16 * len(loads) + 1)
            signal(a, a.activation(k.alog[:], k.alog[:], ACT.Exp), s_a, 1)

        @st.block.gpsimd
        def _(g):
            own = Counter(g, s_c)
            own(g.memset(k.ones[:], 1.0))
            own(g.memset(k.avg[:], 1.0 / P))
            own(g.memset(k.eps[:], 1e-5))
            own(g.memset(k.ident[:], 0.0))
            own(g.affine_select(out=k.ident[:], in_=k.ident[:], compare_op=ALU.not_equal, fill=1.0, base=0,
                                pattern=[[-1, P]], channel_multiplier=1))
            own(g.affine_select(out=k.nident[:], in_=k.ones[:], compare_op=ALU.not_equal, fill=0.0, base=0,
                                pattern=[[-1, P]], channel_multiplier=1))
            own(g.memset(k.gsel[:], 0.0))
            own(g.memset(k.sel[:], 0.0))
            for part in range(3):
                own(g.affine_select(out=k.sel[:], in_=k.sel[:], compare_op=ALU.not_equal, fill=1.0,
                                    base=-2 * DS * part, pattern=[[-1, 2 * DS], [0, P]], channel_multiplier=1))
                own(g.affine_select(out=k.gsel[:], in_=k.gsel[:], compare_op=ALU.not_equal, fill=1.0,
                                    base=-2 * HEADS * part, pattern=[[-1, 2 * HEADS], [0, P]], channel_multiplier=1))

        @st.block.vector
        def _(v):
            opens(v, s_m, s_copy)
            own = Counter(v, s_own)
            signal(v, v.memset(xr[96:P, full, :], 0.0), s_m, 1)
            v.wait_ge(s_v, 16 * (len(VECS) + 8) + 1)
            v.wait_ge(s_a, 2)
            own(v.tensor_scalar(k.alog[:], k.alog[:], -1.0, None, ALU.mult))
            for e in range(2):
                i, h = (VCOL[f"L2_gnn_{('edge', 'node')[e]}_b{x}h"] for x in "ih")
                own(v.tensor_tensor(k.vec[:, i:i + 2], k.vec[:, i:i + 2], k.vec[:, h:h + 2], ALU.add))
            for part in range(3):
                own(v.tensor_copy(k.wbc[:, :, part * 2 * DS:(part + 1) * 2 * DS], k.wxp[:, :, DR:DR + 2 * DS]))

            for g, n in GROUPS:
                v.wait_ge(s_t, g + 2)
                own(v.tensor_copy(k.XT[:, 4 * g * P:(4 * g + n) * P], ps[:, g, 0:n * P]))
                v.sem_inc(s_copy, 1)
            for g in range((NW + 3) // 4):
                n = min(4, NW - 4 * g)
                v.wait_ge(s_t, 7 + g + 2)
                for q in range(n):
                    j = 4 * g + q
                    rows, width = (DA if j == AT_W2 else P), (DA if j >= AT_W1 else P)
                    own(v.tensor_copy(k.wt[0:rows, j, 0:width], ps[0:rows, g, q * P:q * P + width]))
                v.sem_inc(s_copy, 1)
            v.wait_ge(s_wa, 2)
            own(v.tensor_copy(k.wa[:], small[:]))

        @st.block.tensor
        def _(pe):
            opens(pe, s_t, s_wa)
            pe.wait_ge(s_c, 5)
            pe.wait_ge(s_x, 33)
            for g, n in GROUPS:
                for q in range(n):
                    op = pe.transpose(ps[:, g, q * P:(q + 1) * P], xr[:, 4 * g + q, :], k.ident[:])
                op.then_inc(s_t, 1)
            pe.wait_ge(s_w, 16 * (len(WEIGHTS) + 4) + 1)
            for g in range((NW + 3) // 4):
                pe.wait_ge(s_copy, g + 2)
                for q in range(min(4, NW - 4 * g)):
                    j = 4 * g + q
                    rows, width = (DA if j >= AT_W1 else P), (DA if j == AT_W2 else P)
                    op = pe.transpose(ps[0:width, g, q * P:q * P + rows], wr[0:rows, j, 0:width], k.ident[0:rows, 0:rows])
                op.then_inc(s_t, 1)
            pe.wait_ge(s_copy, 7 + 1 + (AT_GAT + HEADS - 1) // 4 + 1)
            for h in range(HEADS):
                op = pe.matmul(small[:, 2 * h:2 * h + 2], k.wt[:, AT_GAT + h, :], gata[:, h, :], start=True, stop=True)
            op.then_inc(s_wa, 1)


def adjacency_and_gcn(nc, k, adj, adjT):
    with stage(nc, "gcn") as st:
        row = st.sb("row", [P, 2, NP])
        AT = st.sb("AT", [P, 2, T, PW])
        junk = st.sb("junk", [P, NP], BF16)
        pick = st.sb("pick", [P, P])
        ps, acc = st.ps("ps", [P, 7, BANK]), st.ps("acc", [P, 2, PW])
        s_pad, s_own = st.sem("pad"), st.sem("own")
        s_row, s_deg, s_min = st.sems("row", 2), st.sems("deg", 2), st.sems("min", 2)
        s_tr, s_ev = st.sems("tr", 7), st.sems("ev", 7)
        s_acc, s_agg, s_diag, s_store = st.sems("acc", 2), st.sems("agg", 2), st.sems("diag", 2), st.sems("store", 2)

        @st.block.sync
        def _(sp):
            opens(sp, s_row)
            sp.wait_ge(s_pad, 2)

            def body(i, b):
                c = 2 * i + b
                for r in range(2):
                    sp.wait_ge(s_tr[6], 2 * c + r + 1)
                    apart(sp)
                    if not (isinstance(c, int) and c == 0):
                        sp.wait_ge(s_deg[r], c + 1)
                        sp.wait_ge(s_min[r], c + 1)
                    if isinstance(c, int) and c == NPC - 1 and r == 1:
                        n = N - (T - 1) * P
                        sp.dma_start(row[0:n, r, 0:N], adj[(T - 1) * P:N, :]).then_inc(s_row[r], 16)
                    else:
                        sp.dma_start(row[:, r, 0:N], adj[ds((2 * c + r) * P, P), :]).then_inc(s_row[r], 16)
            pairs(sp, NPC, body)

        @st.block.gpsimd
        def _(g):
            opens(g, s_pad)
            g.memset(row[:, :, N:NP], 0.0).then_inc(s_pad, 1)

        @st.block.tensor
        def _(pe):
            opens(pe, s_tr, s_acc)
            def body(i, b):
                c = 2 * i + b
                for r in range(2):
                    pe.wait_ge(s_row[r], 16 * (c + 1) + 1)
                    for g, n in GROUPS:
                        pe.wait_ge(s_ev[g], 2 * c + r + 1)
                        for q in range(n):
                            j = 4 * g + q
                            op = pe.transpose(ps[:, g, q * P:(q + 1) * P], row[:, r, j * P:(j + 1) * P], k.ident[:])
                        op.then_inc(s_tr[g], 1)
                for g, _n in GROUPS:
                    pe.wait_ge(s_ev[g], 2 * c + 3)
                pe.wait_ge(s_agg[b], i + 1)
                for j in range(T):
                    op = pe.matmul(acc[:, b, :], k.SW[:, j, :], AT[:, b, j, :], start=j == 0, stop=j == T - 1)
                op.then_inc(s_acc[b], 1)
            pairs(pe, NPC, body)

        def copy_out(eng, i, b, r, who):
            for g, n in GROUPS:
                if g % 2 != who:
                    continue
                eng.wait_ge(s_tr[g], 2 * (2 * i + b) + r + 2)
                out, src = AT[:, b, 4 * g:4 * g + n, r * P:(r + 1) * P], ps[:, g, 0:n * P].rearrange("p (t w) -> p t w", w=P)
                op = eng.tensor_copy(out, src) if who == 0 else eng.activation(out, src, ACT.Copy)
                signal(eng, op, s_ev[g], 2 * (2 * i + b) + r + 1)

        @st.block.vector
        def _(v):
            opens(v, s_min, s_diag, s_ev[0::2])
            own = Counter(v, s_own)

            def body(i, b):
                c = 2 * i + b
                v.wait_ge(s_store[b], 16 * i + 1)
                for r in range(2):
                    copy_out(v, i, b, r, 0)
                    v.wait_ge(s_row[r], 16 * (c + 1) + 1)
                    signal(v, v.tensor_reduce(k.least[:, ds(2 * c + r, 1)], row[:, r, :], AX, ALU.min), s_min[r], c + 1)
                v.wait_ge(s_acc[b], i + 2)
                for r in range(2):
                    block = AT[:, b, ds(2 * c + r, 1), r * P:(r + 1) * P].rearrange("p o w -> p (o w)")
                    own(v.scalar_tensor_tensor(pick[:], block, 1.0, k.ident[:], ALU.mult, ALU.mult,
                                               accum_out=k.dn[:, ds(2 * c + r, 1)]))
                    signal(v, v.tensor_tensor(block, block, k.ident[:], ALU.add), s_diag[b], 2 * i + r + 1)
            with own.loop(NPC // 2, 4) as i:
                body(i, 0)
                body(i, 1)
            body(NPC // 2, 0)

        @st.block.scalar
        def _(a):
            opens(a, s_deg, s_agg, s_store, s_ev[1::2])
            def body(i, b):
                c = 2 * i + b
                a.wait_ge(s_store[b], 16 * i + 1)
                for r in range(2):
                    copy_out(a, i, b, r, 1)
                    a.wait_ge(s_row[r], 16 * (c + 1) + 1)
                    signal(a, a.activation(junk[:], row[:, r, :], ACT.Copy, accum_out=k.deg[:, ds(2 * c + r, 1)]),
                           s_deg[r], c + 1)
                a.wait_ge(s_acc[b], i + 2)
                signal(a, a.activation(k.OT[:, ds(c * PW, PW)], acc[:, b, :], ACT.Relu,
                                       bias=k.vec[:, VCOL["L0_gnn_gcn_b"]:VCOL["L0_gnn_gcn_b"] + 1]), s_agg[b], i + 1)
                a.wait_ge(s_diag[b], 2 * (i + 1) + 1)
                a.dma_start(adjT[ds(c, 1)].rearrange("o p t w -> p (o t) w"), AT[:, b]).then_inc(s_store[b], 16)
            pairs(a, NPC, body)
            a.wait_ge(s_store[0], 16 * ((NPC + 1) // 2) + 1)
            a.wait_ge(s_store[1], 16 * (NPC // 2) + 1)


def inspect_adjacency(nc, k):
    with stage(nc, "inspect") as st:
        root, low, rowlow = st.sb("root", [P, T]), st.sb("low", [P, 1]), st.sb("rowlow", [1, 1])
        ps = st.ps("ps", [1, P])
        s_deg, s_root, s_low, s_t, s_own = st.sem("deg"), st.sem("root"), st.sem("low"), st.sem("t"), st.sem("own")

        @st.block.vector
        def _(v):
            opens(v, s_deg, s_low)
            own = Counter(v, s_own)
            signal(v, v.tensor_scalar(k.deg[:], k.deg[:], 1.0, None, ALU.add), s_deg, 1)
            signal(v, v.tensor_reduce(low[:], k.least[:], AX, ALU.min), s_low, 1)
            own(v.reciprocal(k.rdeg[:], k.deg[:]))
            v.wait_ge(s_root, 2)
            own(v.reciprocal(k.dinv[:], root[:]))
            v.wait_ge(s_t, 2)
            own(v.tensor_reduce(rowlow[:], ps[:], AX, ALU.min))
            own(v.tensor_scalar(k.negative[:], rowlow[:], 0.0, None, ALU.is_lt))

        @st.block.scalar
        def _(a):
            opens(a, s_root)
            a.wait_ge(s_deg, 2)
            signal(a, a.activation(root[:], k.deg[:], ACT.Sqrt), s_root, 1)

        @st.block.tensor
        def _(pe):
            opens(pe, s_t)
            pe.wait_ge(s_low, 2)
            pe.transpose(ps[:], low[:], k.ident[:]).then_inc(s_t, 1)


def mamba_inputs(nc, k):
    with stage(nc, "min") as st:
        xc = st.sb("xc", [P, 2, CW + 3])
        cv, ab, ex, ln, pos = (st.sb(w, [P, 2, CW]) for w in ("cv", "ab", "ex", "ln", "pos"))
        dr = st.sb("dr", [DR, CW])
        r1, r2 = st.sb("r1", [6 * DS, CW]), st.sb("r2", [6 * DS, CW])
        xz, dp = st.ps("xz", [P, 4, BANK]), st.ps("dp", [P, 2, BANK])
        bc, drp = st.ps("bc", [6 * DS, CW]), st.ps("drp", [DR, CW])
        s_xz, s_free, s_halo, s_cv, s_u, s_bc, s_parts = (st.sem(w) for w in ("xz", "free", "halo", "cv", "u", "bc", "parts"))
        s_drp, s_dr, s_dp, s_pos, s_ex, s_out = (st.sem(w) for w in ("drp", "dr", "dp", "pos", "ex", "out"))
        s_own, s_act = st.sem("own"), st.sem("act")
        bdt, cb = VCOL["L0_gnn_b_dt"], VCOL["L0_gnn_conv_b"]

        @st.block.tensor
        def _(pe):
            opens(pe, s_xz, s_bc, s_drp, s_dp)
            with pe.Fori(0, NCH) as i:
                cols = ds(i * CW, CW)
                pe.wait_ge(s_free, 4 * i + 1)
                for m in range(4):
                    pe.matmul(xz[:, m, :CW], k.win[:, m * P:(m + 1) * P], k.OT[:, cols], start=True, stop=True).then_inc(s_xz, 1)
                pe.wait_ge(s_u, 2 * (i + 1) + 1)
                pe.wait_ge(s_parts, i + 1)
                for m in range(2):
                    op = pe.matmul(bc[:], k.wbc[:, m, :], k.U[:, m, cols], start=m == 0, stop=m == 1)
                op.then_inc(s_bc, 1)
                pe.wait_ge(s_dr, i + 1)
                apart(pe)
                for m in range(2):
                    op = pe.matmul(drp[:], k.wxp[:, m, 0:DR], k.U[:, m, cols], start=m == 0, stop=m == 1)
                op.then_inc(s_drp, 1)
                pe.wait_ge(s_dr, i + 2)
                pe.wait_ge(s_pos, 2 * i + 1)
                pe.wait_ge(s_ex, i + 1)
                for m in range(2):
                    op = pe.matmul(dp[:, m, :CW], k.wdt[:, m * P:(m + 1) * P], dr[:], start=True, stop=True)
                op.then_inc(s_dp, 1)

        @st.block.scalar
        def _(a):
            opens(a, s_free, s_u, s_dr, s_ex)
            own = Counter(a, s_act)
            with own.loop(NCH, 4) as i:
                cols = ds(i * CW, CW)
                a.wait_ge(s_halo, i + 2)
                for m in range(2):
                    a.wait_ge(s_xz, 4 * i + m + 2)
                    signal(a, a.activation(xc[:, m, 3:], xz[:, m, :CW], ACT.Copy), s_free, 4 * i + m + 1)
                for m in range(2):
                    a.wait_ge(s_xz, 4 * i + m + 4)
                    signal(a, a.activation(k.ZS[:, m, cols], xz[:, 2 + m, :CW], ACT.Silu), s_free, 4 * i + m + 3)
                for m in range(2):
                    a.wait_ge(s_cv, 2 * i + m + 2)
                    signal(a, a.activation(k.U[:, m, cols], cv[:, m, :], ACT.Silu, bias=k.vec[:, cb + m:cb + m + 1]), s_u, 2 * i + m + 1)
                a.wait_ge(s_drp, i + 2)
                signal(a, a.activation(dr[:], drp[:], ACT.Copy), s_dr, i + 1)
                a.wait_ge(s_dp, i + 2)
                a.wait_ge(s_out, i + 1)
                for m in range(2):
                    own(a.activation(ab[:, m, :], dp[:, m, :CW], ACT.Abs, bias=k.vec[:, bdt + m:bdt + m + 1]))
                own(a.activation(ex[:], ab[:], ACT.Exp, scale=-1.0))
                own(a.activation(ln[:], ex[:], ACT.Ln, bias=1.0))
                a.sem_inc(s_ex, 1)

        @st.block.vector
        def _(v):
            opens(v, s_halo, s_cv, s_parts, s_pos, s_out)
            own = Counter(v, s_own)
            signal(v, v.memset(xc[:, :, 0:3], 0.0), s_halo, 1)
            with own.loop(NCH, 13) as i:
                cols = ds(i * CW, CW)
                v.wait_ge(s_free, 4 * i + 3)
                v.wait_ge(s_u, 2 * i + 1)
                for m in range(2):
                    own(v.tensor_scalar(cv[:, m, :], xc[:, m, 0:CW], k.convw[:, m, 0:1], None, ALU.mult))
                    for j in (1, 2, 3):
                        op = v.scalar_tensor_tensor(cv[:, m, :], xc[:, m, j:j + CW], k.convw[:, m, j:j + 1], cv[:, m, :], ALU.mult, ALU.add)
                        if j < 3:
                            own(op)
                    signal(v, op, s_cv, 2 * i + m + 1)
                signal(v, v.tensor_copy(xc[:, :, 0:3], xc[:, :, CW:CW + 3]), s_halo, i + 2)
                v.wait_ge(s_bc, i + 2)
                apart(v)
                own(v.tensor_copy(k.BC[:, cols], bc[:]))
                own(v.tensor_tensor(r1[:], bc[:], k.BC[:, cols], ALU.subtract))
                apart(v)
                own(v.tensor_copy(k.BC[2 * DS:4 * DS, cols], r1[2 * DS:4 * DS]))
                apart(v)
                own(v.tensor_copy(k.BC[4 * DS:, cols], r1[4 * DS:]))
                own(v.tensor_tensor(r2[4 * DS:], r1[4 * DS:], k.BC[4 * DS:, cols], ALU.subtract))
                apart(v)
                signal(v, v.tensor_copy(k.BC[4 * DS:, cols], r2[4 * DS:]), s_parts, i + 1)
                v.wait_ge(s_ex, i + 2)
                for m in range(2):
                    signal(v, v.tensor_scalar(pos[:, m, :], dp[:, m, :CW], k.vec[:, bdt + m:bdt + m + 1], 0.0, ALU.add, ALU.max), s_pos, 2 * i + m + 1)
                own(v.tensor_tensor(k.DT[:, :, cols], pos[:], ln[:], ALU.add))
                own(v.tensor_tensor(k.DTU[:, :, cols], k.DT[:, :, cols], k.U[:, :, cols], ALU.mult))
                v.sem_inc(s_out, 1)


def mamba_scan(nc, k):
    with stage(nc, "scan") as st:
        dA, dB, H = (st.sb(w, [P, 2, 2, CW]) for w in ("dA", "dB", "H"))
        last = st.sb("last", [P, DS, 2])
        HC = k.HT[:, 0:4 * CW].rearrange("p (a b c) -> p a b c", a=2, b=2)
        yz = k.HT[:, 4 * CW:6 * CW].rearrange("p (b c) -> p b c", b=2)
        bb, cc = st.ps("bb", [P, 2, BANK]), st.ps("cc", [P, 2, BANK])
        y, wo = st.ps("y", [P, 2, BANK]), st.ps("wo", [P, BANK])
        s_bb, s_cc, s_dA, s_scan, s_dB, s_hc, s_y = (st.sems(w, 2) for w in ("bb", "cc", "dA", "scan", "dB", "hc", "y"))
        s_yz, s_wo, s_xt, s_own = st.sem("yz"), st.sem("wo"), st.sem("xt"), st.sem("own")
        HALF = DS // 2
        skip = VCOL["L0_gnn_D_skip"]

        @st.block.tensor
        def _(pe):
            opens(pe, s_bb, s_cc, s_y, s_wo)
            with pe.Fori(0, NCH) as i:
                cols = ds(i * CW, CW)

                def spread_b_c(n):
                    b, u = n % 2, i * HALF + n // 2
                    pe.wait_ge(s_dB[b], u + 1)
                    pe.matmul(bb[:, b, :CW], k.sel[:, n, :], k.BC[:, cols], start=True, stop=True).then_inc(s_bb[b], 1)
                    pe.wait_ge(s_hc[b], u + 1)
                    pe.matmul(cc[:, b, :CW], k.sel[:, DS + n, :], k.BC[:, cols], start=True, stop=True).then_inc(s_cc[b], 1)
                spread_b_c(0)
                for n in range(DS):
                    if n + 1 < DS:
                        spread_b_c(n + 1)
                    if n == 0:
                        pe.wait_ge(s_yz, i + 1)
                    pe.wait_ge(s_hc[n % 2], i * HALF + n // 2 + 2)
                    for m in range(2):
                        op = pe.matmul(y[:, m, :CW], k.ident[:], HC[:, n % 2, m, :], start=n == 0, stop=n == DS - 1)
                    op.then_inc(s_y[n % 2], 1)
                pe.wait_ge(s_yz, i + 2)
                pe.wait_ge(s_xt, i + 1)
                for m in range(2):
                    op = pe.matmul(wo[:, :CW], k.wout[:, m, :], yz[:, m, :], start=m == 0, stop=m == 1)
                op.then_inc(s_wo, 1)

        @st.block.scalar
        def _(a):
            opens(a, s_dA)
            with a.Fori(0, NCH) as i:
                cols = ds(i * CW, CW)
                for n in range(DS):
                    b, u = n % 2, i * HALF + n // 2
                    a.wait_ge(s_scan[b], u + 1)
                    apart(a)
                    a.activation(dA[:, b, 0, :], k.DT[:, 0, cols], ACT.Exp, scale=k.alog[:, 0, n:n + 1]).then_inc(s_dA[b], 1)
                    a.activation(dA[:, b, 1, :], k.DT[:, 1, cols], ACT.Exp, scale=k.alog[:, 1, n:n + 1]).then_inc(s_dA[b], 1)

        @st.block.vector
        def _(v):
            opens(v, s_dB, s_scan, s_hc, s_yz, s_xt)
            own = Counter(v, s_own)
            own(v.memset(last[:], 0.0))
            with own.loop(NCH, 2 * DS + 2) as i:
                cols = ds(i * CW, CW)
                for n in range(DS):
                    b, u = n % 2, i * HALF + n // 2
                    v.wait_ge(s_bb[b], u + 2)
                    signal(v, v.tensor_tensor(dB[:, b], k.DTU[:, :, cols], bb[:, b:b + 1, :CW].to_broadcast([P, 2, CW]), ALU.mult), s_dB[b], u + 1)
                    v.wait_ge(s_dA[b], 2 * (u + 1) + 1)
                    own(v.tensor_tensor_scan(H[:, b, 0, :], dA[:, b, 0, :], dB[:, b, 0, :], last[:, n, 0:1], ALU.mult, ALU.add))
                    signal(v, v.tensor_tensor_scan(H[:, b, 1, :], dA[:, b, 1, :], dB[:, b, 1, :], last[:, n, 1:2], ALU.mult, ALU.add), s_scan[b], u + 1)
                    own(v.tensor_copy(last[:, n, :], H[:, b, :, CW - 1]))
                    v.wait_ge(s_cc[b], u + 2)
                    v.wait_ge(s_y[b], u + 1)
                    signal(v, v.tensor_tensor(HC[:, b], H[:, b], cc[:, b:b + 1, :CW].to_broadcast([P, 2, CW]), ALU.mult), s_hc[b], u + 1)
                for b in range(2):
                    v.wait_ge(s_y[b], (i + 1) * HALF + 1)
                v.wait_ge(s_wo, i + 1)
                for m in range(2):
                    own(v.scalar_tensor_tensor(yz[:, m, :], k.U[:, m, cols], k.vec[:, skip + m:skip + m + 1], y[:, m, :CW], ALU.mult, ALU.add))
                signal(v, v.tensor_tensor(yz, yz, k.ZS[:, :, cols], ALU.mult), s_yz, i + 1)
                v.wait_ge(s_wo, i + 2)
                signal(v, v.tensor_tensor(k.XT[:, cols], k.XT[:, cols], wo[:, :CW], ALU.add), s_xt, i + 1)


def adjacency_pass(nc, k, name, adjT, finish, per, signs=None):
    with stage(nc, name) as st:
        AT = st.sb("AT", [P, 2, T, PW])
        acc = st.ps("acc", [P, 2, BANK])
        if signs:
            mask = st.sb("mask", [P, 2, T, PW], BF16)
            sacc = st.ps("sacc", [18, 2, BANK])
            s_mask, s_sacc, s_sout = st.sems("mask", 2), st.sems("sacc", 2), st.sems("sout", 2)
        s_load, s_clear, s_acc, s_out = st.sems("load", 2), st.sems("clear", 2), st.sems("acc", 2), st.sems("out", 2)
        s_own = st.sem("own")

        @st.block.sync
        def _(sp):
            opens(sp, s_load)
            def body(i, b):
                sp.wait_ge(s_acc[b], i + 1)
                if signs:
                    apart(sp)
                    sp.wait_ge(s_mask[0], 2 * i + b + 1)
                    sp.wait_ge(s_mask[1], 2 * i + b + 1)
                sp.dma_start(AT[:, b], adjT[ds(2 * i + b, 1)].rearrange("o p t w -> p (o t) w")).then_inc(s_load[b], 16)
            pairs(sp, NPC, body)

        @st.block.tensor
        def _(pe):
            opens(pe, s_acc, *([s_sacc] if signs else []))
            def body(i, b):
                c = 2 * i + b
                if signs:
                    pe.wait_ge(s_clear[b], 2 * (i + 1) + 1)
                else:
                    pe.wait_ge(s_load[b], 16 * (i + 1) + 1)
                pe.wait_ge(s_out[b], i + 1)
                for j in range(T):
                    op = pe.matmul(acc[:, b, :PW], k.SW[:, j, :], AT[:, b, j, :], start=j == 0, stop=j == T - 1)
                op.then_inc(s_acc[b], 1)
                if signs:
                    for s in range(2):
                        pe.wait_ge(s_mask[s], c + 2)
                        pe.wait_ge(s_sout[s], c + 1)
                        for j in range(T):
                            op = pe.matmul(sacc[:, s, :PW], k.V3[:, j, :], mask[:, s, j, :], start=j == 0, stop=j == T - 1)
                        op.then_inc(s_sacc[s], 1)
            pairs(pe, NPC, body)

        @st.block.vector
        def _(v):
            opens(v, s_clear, s_out, *([s_mask] if signs else []))
            own = Counter(v, s_own)

            def body(i, b):
                c = 2 * i + b
                if signs:
                    v.wait_ge(s_load[b], 16 * (i + 1) + 1)
                    for r in range(2):
                        block = AT[:, b, ds(2 * c + r, 1), r * P:(r + 1) * P].rearrange("p o w -> p (o w)")
                        signal(v, v.tensor_tensor(block, block, k.nident[:], ALU.mult), s_clear[b], 2 * i + r + 1)
                    for s, op in ((0, ALU.is_gt), (1, ALU.is_lt)):
                        v.wait_ge(s_sacc[s], c + 1)
                        signal(v, v.tensor_scalar(mask[:, s], AT[:, b], 0.0, None, op), s_mask[s], c + 1)
                v.wait_ge(s_acc[b], i + 2)
                finish(v, own, acc[:, b, :PW], ds(c * PW, PW), lambda op: signal(v, op, s_out[b], i + 1))
            if per:
                with own.loop(NPC // 2, 2 * per) as i:
                    body(i, 0)
                    body(i, 1)
                body(NPC // 2, 0)
            else:
                pairs(v, NPC, body)

        if signs:
            @st.block.scalar
            def _(a):
                opens(a, s_sout)
                def body(i, b):
                    c = 2 * i + b
                    for s in range(2):
                        a.wait_ge(s_sacc[s], c + 2)
                        signal(a, a.activation(signs[s][:, ds(c * PW, PW)], sacc[:, s, :PW], ACT.Copy), s_sout[s], c + 1)
                pairs(a, NPC, body)


def gru(nc, k, name, sup, w, bi, bh, weight):
    with stage(nc, name) as st:
        ps = st.ps("ps", [P, 2, 4, BANK])
        rg, zg, nt, ng, o = (st.sb(x, [P, 2, CW]) for x in ("r", "z", "nt", "ng", "o"))
        s_ps, s_rz, s_nt, s_n, s_out = (st.sems(x, 2) for x in ("ps", "rz", "nt", "n", "out"))
        s_own = st.sem("own")

        def cols(i, b):
            return ds((2 * i + b) * CW, CW)

        @st.block.tensor
        def _(pe):
            opens(pe, s_ps)
            with pe.Fori(0, NCH // 2) as i:
                for b in range(2):
                    pe.wait_ge(s_rz[b], 2 * i + 1)
                    pe.wait_ge(s_nt[b], i + 1)
                    for g in range(2):
                        pe.matmul(ps[:, b, g, :CW], k.wt[:, w + g, :], sup[:, cols(i, b)], start=True, stop=False)
                        pe.matmul(ps[:, b, g, :CW], k.wt[:, w + 3 + g, :], k.HT[:, cols(i, b)], start=False, stop=True)
                    pe.matmul(ps[:, b, 2, :CW], k.wt[:, w + 2, :], sup[:, cols(i, b)], start=True, stop=True)
                    pe.matmul(ps[:, b, 3, :CW], k.wt[:, w + 5, :], k.HT[:, cols(i, b)], start=True, stop=True).then_inc(s_ps[b], 1)

        @st.block.scalar
        def _(a):
            opens(a, s_rz, s_n)
            with a.Fori(0, NCH // 2) as i:
                for b in range(2):
                    a.wait_ge(s_ps[b], i + 2)
                    a.wait_ge(s_out[b], i + 1)
                    signal(a, a.activation(rg[:, b], ps[:, b, 0, :CW], ACT.Sigmoid, bias=k.vec[:, bi:bi + 1]), s_rz[b], 2 * i + 1)
                    signal(a, a.activation(zg[:, b], ps[:, b, 1, :CW], ACT.Sigmoid, bias=k.vec[:, bi + 1:bi + 2]), s_rz[b], 2 * i + 2)
                for b in range(2):
                    a.wait_ge(s_nt[b], i + 2)
                    signal(a, a.activation(ng[:, b], nt[:, b], ACT.Tanh, bias=k.vec[:, bi + 2:bi + 3]), s_n[b], i + 1)

        @st.block.vector
        def _(v):
            opens(v, s_nt, s_out)
            own = Counter(v, s_own)
            with own.loop(NCH // 2, 10) as i:
                for b in range(2):
                    v.wait_ge(s_rz[b], 2 * i + 2)
                    v.wait_ge(s_n[b], i + 1)
                    own(v.scalar_tensor_tensor(nt[:, b], ps[:, b, 3, :CW], k.vec[:, bh + 2:bh + 3], rg[:, b], ALU.add, ALU.mult))
                    signal(v, v.tensor_tensor(nt[:, b], nt[:, b], ps[:, b, 2, :CW], ALU.add), s_nt[b], i + 1)
                for b in range(2):
                    v.wait_ge(s_n[b], i + 2)
                    v.wait_ge(s_rz[b], 2 * i + 3)
                    own(v.tensor_tensor(o[:, b], k.HT[:, cols(i, b)], ng[:, b], ALU.subtract))
                    own(v.tensor_tensor(o[:, b], o[:, b], zg[:, b], ALU.mult))
                    own(v.tensor_tensor(o[:, b], o[:, b], ng[:, b], ALU.add))
                    own(v.tensor_tensor(o[:, b], o[:, b], weight[:, cols(i, b)], ALU.mult))
                    signal(v, v.tensor_tensor(k.XT[:, cols(i, b)], k.XT[:, cols(i, b)], o[:, b], ALU.add), s_out[b], i + 1)


def split_gat_vectors(nc, k, V):
    with stage(nc, "split") as st:
        rest = st.sb("rest", [P, T, 6])
        s_own = st.sem("own")

        @st.block.vector
        def _(v):
            own = Counter(v, s_own)
            for part in range(3):
                own(v.tensor_copy(k.V3[:, :, 6 * part:6 * part + 6], V[:]))
                own(v.tensor_tensor(rest[:], V[:], k.V3[:, :, 6 * part:6 * part + 6], ALU.subtract))
                own(v.tensor_copy(V[:], rest[:]))


def attention_logits(nc, k, h, Gp, Gm, E):
    with stage(nc, f"elog{h}") as st:
        ps = st.ps("ps", [P, 2, 2, BANK])
        s_ps, s_out = st.sems("ps", 2), st.sems("out", 2)

        @st.block.tensor
        def _(pe):
            opens(pe, s_ps)
            with pe.Fori(0, NCH // 2) as i:
                for b in range(2):
                    cols = ds((2 * i + b) * CW, CW)
                    pe.wait_ge(s_out[b], 2 * i + 1)
                    for s, (x, y) in enumerate(((Gp, Gm), (Gm, Gp))):
                        pe.matmul(ps[:, b, s, :CW], k.gsel[:, 2 * h, :], x[:, cols], start=True, stop=False)
                        op = pe.matmul(ps[:, b, s, :CW], k.gsel[:, 2 * h + 1, :], y[:, cols], start=False, stop=True)
                    op.then_inc(s_ps[b], 1)

        @st.block.vector
        def _(v):
            opens(v, s_out)
            own = Counter(v, st.sem("own"))
            with own.loop(NCH // 2, 4) as i:
                for b in range(2):
                    cols = ds((2 * i + b) * CW, CW)
                    v.wait_ge(s_ps[b], i + 2)
                    for s in range(2):
                        own(v.tensor_scalar(E[:, s, cols], ps[:, b, s, :CW], 0.2, None, ALU.mult))
                        signal(v, v.tensor_tensor(E[:, s, cols], E[:, s, cols], ps[:, b, s, :CW], ALU.max), s_out[b], 2 * i + s + 1)


def attention_head(nc, k, h, adj, E, SUP):
    with stage(nc, f"head{h}") as st:
        row, L = st.sb("row", [P, 2, NP]), st.sb("L", [P, 2, NP])
        NM, PT = st.sb("NM", [P, NP]), st.sb("PT", [P, T, P])
        ml, rs = st.sb("ml", [P, 2]), st.sb("rs", [P, 2, 2])
        ps, acc = st.ps("ps", [P, 7, BANK]), st.ps("acc", [P, P])
        s_pad, s_own = st.sem("pad"), st.sem("own")
        s_row, s_L, s_P, s_PA = (st.sems(w, 2) for w in ("row", "L", "P", "PA"))
        s_tr, s_ev = st.sems("tr", 7), st.sem("ev")
        s_acc, s_sup = st.sem("acc"), st.sem("sup")
        HT2 = T // 2

        @st.block.gpsimd
        def _(g):
            opens(g, s_pad)
            g.memset(row[:, :, N:NP], 0.0).then_inc(s_pad, 1)

        @st.block.sync
        def _(sp):
            opens(sp, s_row)
            sp.wait_ge(s_pad, 2)

            def body(i):
                for b in range(2):
                    sp.wait_ge(s_PA[b], i + 1)
                    if isinstance(i, int) and b == 1:
                        n = N - (T - 1) * P
                        sp.dma_start(row[0:n, b, 0:N], adj[(T - 1) * P:N, :]).then_inc(s_row[b], 16)
                    else:
                        sp.dma_start(row[:, b, 0:N], adj[ds((2 * i + b) * P, P), :]).then_inc(s_row[b], 16)
            with sp.Fori(0, HT2 - 1) as i:
                body(i)
            body(HT2 - 1)

        @st.block.vector
        def _(v):
            opens(v, s_L, s_PA, s_sup)
            own = Counter(v, s_own)
            negative = v.value_load(k.negative[0:1, 0:1])
            with own.loop(HT2, 8) as i:
                for b in range(2):
                    block = row[:, b, ds((2 * i + b) * P, P)]
                    v.wait_ge(s_row[b], 16 * (i + 1) + 1)
                    own(v.tensor_tensor(block, block, k.nident[:], ALU.mult))
                    own(v.tensor_scalar(NM[:], row[:, b, :], 0.0, MASKED, ALU.is_le, ALU.mult))
                    v.wait_ge(s_PA[b], i + 1)
                    v.wait_ge(s_tr[6], 2 * i + 1)
                    apart(v)
                    own(v.tensor_tensor_reduce(out=L[:, b, :], in0=NM[:], in1=E[:, 0, :], scale=1.0, scalar=-3e38,
                                               op0=ALU.add, op1=ALU.max, accum_out=ml[:, b:b + 1]))
                    apart(v)
                    with v.If(negative != 0):
                        v.tensor_scalar(NM[:], row[:, b, :], 0.0, MASKED, ALU.is_ge, ALU.mult)
                        v.drain()
                        v.tensor_tensor(NM[:], NM[:], E[:, 1, :], ALU.add)
                        v.drain()
                        v.tensor_tensor(L[:, b, :], L[:, b, :], NM[:], ALU.max)
                        v.drain()
                        v.tensor_reduce(ml[:, b:b + 1], L[:, b, :], AX, ALU.max)
                        v.drain()
                    signal(v, v.tensor_scalar(ml[:, b:b + 1], ml[:, b:b + 1], -1.0, None, ALU.mult), s_L[b], i + 1)
                for b in range(2):
                    v.wait_ge(s_P[b], i + 2)
                    own(v.reciprocal(rs[:, b, 1:2], rs[:, b, 0:1]))
                    signal(v, v.scalar_tensor_tensor(L[:, b, :], L[:, b, :], rs[:, b, 1:2], row[:, b, :], ALU.mult, ALU.mult), s_PA[b], i + 1)
                    v.wait_ge(s_acc, 2 * i + b + 2)
                    cols = ds((2 * i + b) * P, P)
                    if h:
                        op = v.tensor_tensor(SUP[:, cols], SUP[:, cols], acc[:], ALU.add)
                    else:
                        op = v.tensor_copy(SUP[:, cols], acc[:])
                    signal(v, op, s_sup, 2 * i + b + 1)

        @st.block.scalar
        def _(a):
            opens(a, s_P, s_ev)
            with a.Fori(0, HT2) as i:
                def exps(b):
                    a.wait_ge(s_L[b], i + 2)
                    signal(a, a.activation(L[:, b, :], L[:, b, :], ACT.Exp, bias=ml[:, b:b + 1], accum_out=rs[:, b, 0:1]), s_P[b], i + 1)
                exps(0)
                exps(1)
                for b in range(2):
                    a.wait_ge(s_acc, 2 * i + b + 1)
                    for g, n in GROUPS:
                        a.wait_ge(s_tr[g], 2 * i + b + 2)
                        signal(a, a.activation(PT[:, 4 * g:4 * g + n, :], ps[:, g, 0:n * P].rearrange("p (t w) -> p t w", w=P), ACT.Copy),
                               s_ev, (2 * i + b) * 7 + g + 1)

        @st.block.tensor
        def _(pe):
            opens(pe, s_tr, s_acc)
            with pe.Fori(0, HT2) as i:
                for b in range(2):
                    pe.wait_ge(s_PA[b], i + 2)
                    pe.wait_ge(s_ev, (2 * i + b) * 7 + 1)
                    for g, n in GROUPS:
                        for q in range(n):
                            j = 4 * g + q
                            op = pe.transpose(ps[:, g, q * P:(q + 1) * P], L[:, b, j * P:(j + 1) * P], k.ident[:])
                        op.then_inc(s_tr[g], 1)
                    pe.wait_ge(s_sup, 2 * i + b + 1)
                    pe.wait_ge(s_ev, (2 * i + b + 1) * 7 + 1)
                    for j in range(T):
                        op = pe.matmul(acc[:], k.SW[:, j, :], PT[:, j, :], start=j == 0, stop=j == T - 1)
                    op.then_inc(s_acc, 1)


def queries_and_keys(nc, k, name, src, QT, KT):
    with stage(nc, name) as st:
        ps = st.ps("ps", [P, 3, BANK])
        q1 = st.sb("q1", [DA, CW])
        s_a, s_q1, s_q, s_copy = st.sem("a"), st.sem("q1"), st.sem("q"), st.sem("copy")

        @st.block.tensor
        def _(pe):
            opens(pe, s_a, s_q)
            with pe.Fori(0, NCH) as i:
                cols = ds(i * CW, CW)
                pe.wait_ge(s_copy, 2 * i + 1)
                pe.matmul(ps[0:DA, 0, :CW], k.wt[:, AT_W1, 0:DA], src[:, cols], start=True, stop=True)
                pe.matmul(ps[0:DA, 1, :CW], k.wt[:, AT_W3, 0:DA], src[:, cols], start=True, stop=True).then_inc(s_a, 1)
                pe.wait_ge(s_q1, i + 2)
                apart(pe)
                pe.matmul(ps[0:DA, 2, :CW], k.wt[0:DA, AT_W2, 0:DA], q1[:], start=True, stop=True).then_inc(s_q, 1)

        @st.block.scalar
        def _(a):
            opens(a, s_q1, s_copy)
            with a.Fori(0, NCH) as i:
                cols = ds(i * CW, CW)
                a.wait_ge(s_a, i + 2)
                signal(a, a.activation(q1[:], ps[0:DA, 0, :CW], ACT.Copy), s_q1, i + 1)
                signal(a, a.activation(KT[:, cols], ps[0:DA, 1, :CW], ACT.Copy), s_copy, 2 * i + 1)
                a.wait_ge(s_q, i + 2)
                signal(a, a.activation(QT[:, cols], ps[0:DA, 2, :CW], ACT.Copy), s_copy, 2 * i + 2)


def top_p_attention(nc, k, name, QT, KT, X, Y):
    LOWEST = -10.43
    WIDTH = 10.5
    with stage(nc, name) as st:
        Z, E = st.sb("Z", [P, 2, NP]), st.sb("E", [P, 2, NP])
        PT, qs, junk = st.sb("PT", [P, T, P]), st.sb("qs", [DA, 2, P]), st.sb("junk", [P, NP], BF16)
        mx, nmx, S, lo, cand, mass, step, goal, rm, ge = (
            st.sb(w, [P, 2]) for w in ("mx", "nmx", "S", "lo", "cand", "mass", "step", "goal", "rm", "ge"))
        lg, ps, acc = st.ps("lg", [P, 4, BANK]), st.ps("ps", [P, 3, BANK]), st.ps("acc", [P, P])
        s_q, s_lg, s_z, s_max, s_E, s_A = (st.sems(w, n) for w, n in (("q", 2), ("lg", 4), ("z", 4), ("max", 2), ("E", 2), ("A", 2)))
        s_tr, s_ev, s_acc, s_y, s_own = st.sem("tr"), st.sem("ev"), st.sem("acc"), st.sem("y"), st.sem("own")
        H2 = T // 2

        @st.block.tensor
        def _(pe):
            opens(pe, s_lg, s_tr, s_acc)
            with pe.Fori(0, H2) as i:
                for b in range(2):
                    pe.wait_ge(s_q[b], i + 2)
                    for j in range(NCH):
                        m = j % 4
                        pe.wait_ge(s_z[m], 2 * (2 * i + b) + j // 4 + 1)
                        pe.matmul(lg[:, m, :CW], qs[:, b, :], KT[:, j * CW:(j + 1) * CW], start=True, stop=True).then_inc(s_lg[m], 1)
                for b in range(2):
                    u = 2 * i + b
                    pe.wait_ge(s_A[b], i + 2)
                    for g, n in GROUPS:
                        pe.wait_ge(s_ev, 7 * u + max(0, g - 2) + 1)
                        for q in range(n):
                            j = 4 * g + q
                            op = pe.transpose(ps[:, g % 3, q * P:(q + 1) * P], E[:, b, j * P:(j + 1) * P], k.ident[:])
                        op.then_inc(s_tr, 1)
                    pe.wait_ge(s_y, u + 1)
                    pe.wait_ge(s_ev, 7 * (u + 1) + 1)
                    for j in range(T):
                        op = pe.matmul(acc[:], PT[:, j, :], X[:, j, :], start=j == 0, stop=j == T - 1)
                    op.then_inc(s_acc, 1)

        @st.block.scalar
        def _(a):
            opens(a, s_q, s_z, s_E, s_ev, s_y)
            with a.Fori(0, H2) as i:
                for b in range(2):
                    u = 2 * i + b
                    a.wait_ge(s_lg[3], 4 * i + 1)
                    signal(a, a.activation(qs[:, b, :], QT[:, ds(u * P, P)], ACT.Copy), s_q[b], i + 1)
                    a.wait_ge(s_A[b], i + 1)
                    for j in range(NCH):
                        m = j % 4
                        a.wait_ge(s_lg[m], 2 * u + j // 4 + 2)
                        signal(a, a.activation(Z[:, b, j * CW:(j + 1) * CW], lg[:, m, :CW], ACT.Copy), s_z[m], 2 * u + j // 4 + 1)
                    a.wait_ge(s_max[b], i + 2)
                    a.wait_ge(s_tr, 14 * i + 1)
                    signal(a, a.activation(E[:, b, 0:N], Z[:, b, 0:N], ACT.Exp, bias=nmx[:, b:b + 1], accum_out=S[:, b:b + 1]), s_E[b], i + 1)
                for b in range(2):
                    u = 2 * i + b
                    a.wait_ge(s_acc, u + 1)
                    for g, n in GROUPS:
                        a.wait_ge(s_tr, 7 * u + g + 2)
                        signal(a, a.activation(PT[:, 4 * g:4 * g + n, :], ps[:, g % 3, 0:n * P].rearrange("p (t w) -> p t w", w=P), ACT.Copy),
                               s_ev, 7 * u + g + 1)
                    a.wait_ge(s_acc, u + 2)
                    signal(a, a.activation(Y[:, ds(u, 1), :].rearrange("p o w -> p (o w)"), acc[:], ACT.Copy, scale=rm[:, b:b + 1]), s_y, u + 1)

        @st.block.vector
        def _(v):
            opens(v, s_max, s_A)
            own = Counter(v, s_own)
            own(v.memset(E[:, :, N:NP], 0.0))
            with own.loop(H2, 2 + 3 + 7 * SEARCH + 4) as i:
                for b in range(2):
                    for m in range(4):
                        v.wait_ge(s_z[m], 2 * (2 * i + b) + 3)
                    own(v.tensor_reduce(mx[:, b:b + 1], Z[:, b, 0:N], AX, ALU.max))
                    signal(v, v.tensor_scalar(nmx[:, b:b + 1], mx[:, b:b + 1], -1.0, None, ALU.mult), s_max[b], i + 1)
                for b in range(2):
                    v.wait_ge(s_E[b], i + 2)
                own(v.tensor_scalar(goal[:], S[:], TOP_P, None, ALU.mult))
                own(v.tensor_scalar(lo[:], mx[:], LOWEST, None, ALU.add))
                own(v.memset(step[:], WIDTH / 2))
                apart(v)
                with own.loop(SEARCH, 7):
                    own(v.tensor_tensor(cand[:], lo[:], step[:], ALU.add))
                    for b in range(2):
                        own(v.scalar_tensor_tensor(junk[:, 0:N], Z[:, b, 0:N], cand[:, b:b + 1], E[:, b, 0:N],
                                                   ALU.is_ge, ALU.mult, accum_out=mass[:, b:b + 1]))
                    own(v.tensor_tensor(ge[:], mass[:], goal[:], ALU.is_ge))
                    own(v.tensor_tensor(ge[:], ge[:], step[:], ALU.mult))
                    own(v.tensor_tensor(lo[:], lo[:], ge[:], ALU.add))
                    own(v.tensor_scalar(step[:], step[:], 0.5, None, ALU.mult))
                for b in range(2):
                    own(v.scalar_tensor_tensor(E[:, b, 0:N], Z[:, b, 0:N], lo[:, b:b + 1], E[:, b, 0:N],
                                               ALU.is_ge, ALU.mult, accum_out=mass[:, b:b + 1]))
                    own(v.tensor_scalar(mass[:, b:b + 1], mass[:, b:b + 1], 1e-12, None, ALU.max))
                    signal(v, v.reciprocal(rm[:, b:b + 1], mass[:, b:b + 1]), s_A[b], i + 1)


def add_products(nc, k, name, terms, Z, first):
    with stage(nc, name) as st:
        ps = st.ps("ps", [P, 2, BANK])
        s_ps, s_out = st.sems("ps", 2), st.sems("out", 2)

        @st.block.tensor
        def _(pe):
            opens(pe, s_ps)
            with pe.Fori(0, NCH // 2) as i:
                for b in range(2):
                    pe.wait_ge(s_out[b], i + 1)
                    for n, (w, x) in enumerate(terms):
                        op = pe.matmul(ps[:, b, :CW], w, x[:, ds((2 * i + b) * CW, CW)], start=n == 0, stop=n == len(terms) - 1)
                    op.then_inc(s_ps[b], 1)

        @st.block.vector
        def _(v):
            opens(v, s_out)
            with v.Fori(0, NCH // 2) as i:
                for b in range(2):
                    cols = ds((2 * i + b) * CW, CW)
                    v.wait_ge(s_ps[b], i + 2)
                    signal(v, v.tensor_tensor(Z[:, cols], first[:, cols], ps[:, b, :CW], ALU.add), s_out[b], i + 1)


def program(nc, d, out, probes=()):
    adjT = nc.dram_tensor("adjT", (NPC, P, T, PW), F32).ap()
    probes = dict(probes)

    def probe(name, buf):
        if name in probes:
            with stage(nc, "probe_" + name) as st:
                s = st.sem("s")

                @st.block.sync
                def _(sp):
                    opens(sp, s)
                    sp.dma_start(probes[name], buf[:]).then_inc(s, 16)
                    sp.wait_ge(s, 17)

    with ExitStack() as ctx:
        def sb(name, shape, dt=F32):
            return ctx.enter_context(nc.sbuf_tensor(name, shape, dt))

        k = Kept()
        k.XT, k.HT, k.OT = sb("XT", [P, NP]), sb("HT", [P, NP]), sb("OT", [P, NP])
        k.ident, k.nident, k.avg, k.ones = (sb(n, [P, P]) for n in ("ident", "nident", "avg", "ones"))
        k.eps, k.vec, k.wt, k.gatw = sb("eps", [P, 1]), sb("vec", [P, NVEC]), sb("wt", [P, NW, P]), sb("gatw", [P, HEADS, P])
        k.wa, k.gsel = sb("wa", [P, 2 * HEADS]), sb("gsel", [18, 6, P])
        k.deg, k.rdeg, k.dinv, k.dn, k.least = (sb(n, [P, T]) for n in ("deg", "rdeg", "dinv", "dn", "least"))
        k.negative = sb("negative", [1, 1], I32)
        with ExitStack() as early:
            def sb1(name, shape, dt=F32):
                return early.enter_context(nc.sbuf_tensor(name, shape, dt))
            k.sel = sb1("sel", [6 * DS, 2 * DS, P], BF16)
            k.convw, k.alog = sb1("convw", [P, 2, 4]), sb1("alog", [P, 2, DS])
            k.gcnw, k.win, k.wxp = sb1("gcnw", [P, P]), sb1("win", [P, 4 * P]), sb1("wxp", [P, 2, DR + 2 * DS])
            k.wbc, k.wdt, k.wout = sb1("wbc", [P, 2, 6 * DS]), sb1("wdt", [DR, DI]), sb1("wout", [P, 2, P])
            setup(nc, k, d)
            layer_norm(nc, k, "ln0", k.XT, k.HT, True)
            with nc.sbuf_tensor("SW0", [P, T, P], F32) as k.SW:
                rows_times(nc, k, "hw0", k.HT, k.gcnw[:], k.SW)
                adjacency_and_gcn(nc, k, d["adj"], adjT)
            inspect_adjacency(nc, k)
            layer_norm(nc, k, "ln1", k.OT, k.OT, False,
                       *(k.vec[:, VCOL[n]:VCOL[n] + 1] for n in ("L0_gnn_ln_g", "L0_gnn_ln_b")))
            with ExitStack() as inner:
                k.U, k.DTU, k.ZS = (inner.enter_context(nc.sbuf_tensor(n, [P, 2, NP], F32)) for n in ("U", "DTU", "ZS"))
                k.DT = inner.enter_context(nc.sbuf_tensor("DT", [P, 2, NP], F32))
                k.BC = inner.enter_context(nc.sbuf_tensor("BC", [6 * DS, NP], BF16))
                mamba_inputs(nc, k)
                mamba_scan(nc, k)
        probe("x1", k.XT)
        k.SW = sb("SW", [P, T, P])
        layer_norm(nc, k, "ln2", k.XT, k.HT, True)
        rows_times(nc, k, "hw1", k.HT, k.wt[:, 0, :], k.SW, scale=lambda t: k.dinv[:, t:t + 1])
        with nc.sbuf_tensor("DB", [P, NP], F32) as DB:
            spread(nc, k, "spread1", k.dinv, DB)

            def gcn_out(v, own, acc, cols, last):
                own(v.tensor_tensor(k.OT[:, cols], acc, DB[:, cols], ALU.mult))
                last(v.scalar_tensor_tensor(k.XT[:, cols], k.OT[:, cols], 0.0, k.XT[:, cols], ALU.max, ALU.add))
            adjacency_pass(nc, k, "gcn1", adjT, gcn_out, 1)
        probe("x2", k.XT)
        layer_norm(nc, k, "ln3", k.XT, k.HT, True)
        with nc.sbuf_tensor("Gp", [18, NP], F32) as Gp, nc.sbuf_tensor("Gm", [18, NP], F32) as Gm:
            with nc.sbuf_tensor("V", [P, T, 6], F32) as V, nc.sbuf_tensor("V3", [P, T, 18], BF16) as k.V3:
                by_tiles(nc, "gatv", lambda pe, o, t: pe.matmul(o, k.HT[:, t * P:(t + 1) * P], k.wa[:], start=True, stop=True),
                         lambda g, n: V[:, 4 * g:4 * g + n, :].rearrange("p t c -> p (t c)"), width=6)
                split_gat_vectors(nc, k, V)
                to_rows(nc, k, "hrows", k.HT, k.SW)
                adjacency_pass(nc, k, "gat", adjT,
                               lambda v, own, acc, cols, last: last(v.tensor_copy(k.OT[:, cols], acc)), 0, signs=(Gp, Gm))
            with nc.sbuf_tensor("DNB", [P, NP], F32) as DNB:
                spread(nc, k, "spread2", k.dn, DNB)
                gru(nc, k, "gru1", k.OT, AT_EDGE, VCOL["L2_gnn_edge_bih"], VCOL["L2_gnn_edge_bhh"], DNB)
            with nc.sbuf_tensor("E2", [P, 2, NP], F32) as E2:
                for h in range(HEADS):
                    rows_times(nc, k, f"hw2{h}", k.HT, k.gatw[:, h, :], k.SW)
                    attention_logits(nc, k, h, Gp, Gm, E2)
                    attention_head(nc, k, h, d["adj"], E2, k.OT)
        with nc.sbuf_tensor("DNB2", [P, NP], F32) as DNB:
            spread(nc, k, "spread3", k.dn, DNB)
            mean_of_heads(nc, k)
            gru(nc, k, "gru2", k.OT, AT_NODE, VCOL["L2_gnn_node_bih"], VCOL["L2_gnn_node_bhh"], DNB)
        probe("x3", k.XT)
        layer_norm(nc, k, "ln4", k.XT, k.HT, True)
        to_rows(nc, k, "hrows2", k.HT, k.SW)
        with nc.sbuf_tensor("ZT", [P, NP], F32) as ZT, nc.sbuf_tensor("Xa", [P, T, P], F32) as Xa:
            src = k.HT
            for n in range(2):
                with nc.sbuf_tensor(f"QT{n}", [DA, NP], F32) as QT, nc.sbuf_tensor(f"KT{n}", [DA, NP], F32) as KT:
                    queries_and_keys(nc, k, f"qk{n}", src, QT, KT)
                    if n == 0:
                        top_p_attention(nc, k, "topp0", QT, KT, k.SW, Xa)
                    else:
                        Xb = k.HT[:].rearrange("p (t d) -> p t d", d=P)
                        top_p_attention(nc, k, "topp1", QT, KT, Xa, Xb)
                with nc.sbuf_tensor(f"RB{n}", [P, NP], F32) as RB:
                    spread(nc, k, f"spread4{n}", k.rdeg, RB)
                    adjacency_pass(nc, k, f"mix{n}", adjT,
                                   lambda v, own, acc, cols, last: last(v.tensor_tensor(k.OT[:, cols], acc, RB[:, cols], ALU.mult)), 0)
                if n == 0:
                    to_rows(nc, k, "xfrows", k.OT, k.SW)
                    with nc.sbuf_tensor("XaT", [P, NP], F32) as XaT:
                        to_cols(nc, k, "xacols0", Xa, XaT)
                        add_products(nc, k, "u0", [(k.wt[:, AT_U1, :], k.OT), (k.wt[:, AT_U2, :], XaT)], ZT, k.HT)
                        copy_all(nc, k, "keep", XaT, k.HT)
                else:
                    with nc.sbuf_tensor("XbT", [P, NP], F32) as XbT:
                        to_cols(nc, k, "xacols1", Xb, XbT)
                        add_products(nc, k, "u1", [(k.wt[:, AT_U1 + 1, :], k.OT), (k.wt[:, AT_U2 + 1, :], XbT)], ZT, ZT)
            layer_norm(nc, k, "ln5", ZT, k.HT, False,
                       *(k.vec[:, VCOL[n]:VCOL[n] + 1] for n in ("L3_gnn_ln_g", "L3_gnn_ln_b")))
        finish(nc, k, out)


def copy_all(nc, k, name, src, dst, scale=1.0):
    with stage(nc, name) as st:
        s = st.sem("s")
        st.block.vector(lambda v: (opens(v, s), signal(v, v.tensor_scalar(dst[:], src[:], scale, None, ALU.mult), s, 1)))


def mean_of_heads(nc, k):
    copy_all(nc, k, "heads", k.OT, k.OT, 1.0 / HEADS)


def finish(nc, k, out):
    with stage(nc, "add") as st:
        s = st.sem("s")
        st.block.vector(lambda v: (opens(v, s), signal(v, v.tensor_tensor(k.XT[:], k.XT[:], k.HT[:], ALU.add), s, 1)))
    to_rows(nc, k, "outrows", k.XT, k.SW)
    with stage(nc, "store") as st:
        s = st.sem("s")
        full = N // P

        @st.block.sync
        def _(sp):
            opens(sp, s)
            sp.dma_start(out[0:full * P, :].rearrange("(t p) d -> p t d", p=P), k.SW[:, 0:full, :]).then_inc(s, 16)
            sp.dma_start(out[full * P:N, :], k.SW[0:N - full * P, full, :]).then_inc(s, 16)
            sp.wait_ge(s, 33)


_INS = ["x", "adj", "L0_gnn_gcn_w", "L0_gnn_gcn_b", "L0_gnn_ln_g", "L0_gnn_ln_b", "L0_gnn_w_in", "L0_gnn_conv_w",
        "L0_gnn_conv_b", "L0_gnn_w_xp", "L0_gnn_w_dt", "L0_gnn_b_dt", "L0_gnn_A_log", "L0_gnn_D_skip", "L0_gnn_w_out",
        "L1_gnn_W", "L2_gnn_gat_W", "L2_gnn_gat_a", "L2_gnn_edge_Wih", "L2_gnn_edge_Whh", "L2_gnn_edge_bih",
        "L2_gnn_edge_bhh", "L2_gnn_node_Wih", "L2_gnn_node_Whh", "L2_gnn_node_bih", "L2_gnn_node_bhh", "L3_gnn_W1",
        "L3_gnn_W2", "L3_gnn_W3", "L3_gnn_U1", "L3_gnn_U2", "L3_gnn_ln_g", "L3_gnn_ln_b"]


def kernel(**inputs):
    import numpy as np
    import concourse.bacc as bacc
    from concourse.bass_utils import run_bass_kernel_spmd

    nc = bacc.Bacc("TRN2", target_bir_lowering=False, num_devices=1)
    arrays, aps = {}, {}
    for name in _INS:
        a = np.ascontiguousarray(inputs[name])
        arrays[f"in_{name}"] = a
        aps[name] = nc.dram_tensor(f"in_{name}", a.shape, mybir.dt.from_np(a.dtype), kind="ExternalInput").ap()
    out = nc.dram_tensor("out", (N, P), F32, kind="ExternalOutput").ap()
    program(nc, aps, out)
    r = run_bass_kernel_spmd(nc, [arrays], core_ids=[0])
    return r.results[0]["out"]
```
